# Optimizing a Trainium2 kernel written in Bass

```python
import numpy as np
import jax
import jax.numpy as jnp

def _softmax(x, axis=-1):
    return jax.nn.softmax(x, axis=axis)

def _gelu(x):
    return jax.nn.gelu(x, approximate=True)

def _silu(x):
    return jax.nn.silu(x)

def _sigmoid(x):
    return jax.nn.sigmoid(x)

def _layernorm(x, axis=-1, eps=1e-05):
    m = jnp.mean(x, axis=axis, keepdims=True)
    v = jnp.var(x, axis=axis, keepdims=True)
    return (x - m) / jnp.sqrt(v + eps)

def _scatter_add(tgt, idx, src, axis=0):
    return tgt.at[idx].add(src)

def _segment_sum(src, seg, n):
    return jax.ops.segment_sum(src, seg, n)
kernel_name = 'mk_cond_resid_d1_seqx_r2_4806c4'

def setup_inputs(seed: int=0):
    np.random.seed(seed)
    _w = jnp.asarray

    def _rec_inputs():
        import jax
        import jax.numpy as jnp
        _rk = jax.random.key(seed)
        x = 0.000341 + 1 * jax.random.normal(jax.random.fold_in(_rk, 1), (4, 1024, 512), jnp.float32)
        _lenS = 1024 - jax.random.randint(jax.random.fold_in(_rk, 7), (4,), 0, max(1, 1024 // 4) + 1, jnp.int32)
        _lenS2 = 1024 - jax.random.randint(jax.random.fold_in(_rk, 8), (4,), 0, max(1, 1024 // 4) + 1, jnp.int32)
        cond_512 = -0.003599 + 1.01223 * jax.random.normal(jax.random.fold_in(_rk, 11), (4, 256), jnp.float32)
        return (x, cond_512)
    x, cond_512 = _rec_inputs()

    def _L0_cond_setup():
        import jax, jax.numpy as jnp
        import numpy as np
        B, L, D = (8, 1024, 512)
        key = jax.random.key(seed)
        k0, k1, k2, k3 = jax.random.split(key, 4)
        hidden0 = jax.random.normal(k0, (B, D // 2), dtype=jnp.float32)
        hidden1 = jax.random.normal(k1, (B, D // 2), dtype=jnp.float32)
        x = jax.random.normal(k2, (B, L, D), dtype=jnp.float32)
        W = jax.random.normal(k3, (3 * D, D), dtype=jnp.float32) * (1.0 / np.sqrt(3 * D))
        b = jnp.zeros((D,), dtype=jnp.float32)
        return {'hidden0': hidden0, 'hidden1': hidden1, 'x': x, 'W': W, 'b': b}
    _L0_cond_all = _L0_cond_setup()
    _L0_cond_in = {k: v for k, v in _L0_cond_all.items() if k in ('W', 'b')}
    del _L0_cond_all
    return {'x': x, 'cond_512': cond_512, 'L0_cond_W': _L0_cond_in['W'], 'L0_cond_b': _L0_cond_in['b']}

def reference(x, cond_512, L0_cond_W, L0_cond_b):
    import jax
    import jax.numpy as jnp

    def _L0_cond_ref(hidden0, hidden1, x, W, b):
        import jax, jax.numpy as jnp
        import numpy as np
        B, L, D = (8, 1024, 512)
        hidden = jnp.concatenate([hidden0, hidden1], axis=-1)
        x_mean = jnp.mean(x, axis=1, keepdims=True)
        ones_L = jnp.ones((1, L, 1), dtype=x.dtype)
        fused = jnp.concatenate([x, x_mean * ones_L, hidden[:, None, :] * ones_L], axis=-1)
        relation = jax.nn.relu(jnp.einsum('bld,do->blo', fused, W) + b)
        return relation
    x = x + _L0_cond_ref(cond_512, cond_512, x, L0_cond_W, L0_cond_b)
    return x

_drawn_inputs = setup_inputs


def setup_inputs(seed=0):
    import zlib

    import numpy as np

    out = dict(_drawn_inputs(seed))
    spreads = {'L0_cond_b': (0.0, 0.1)}
    factors = {}
    for name, (base, spread) in spreads.items():
        noise = np.random.default_rng([zlib.crc32(name.encode()), seed]).standard_normal(out[name].shape)
        drawn = base * np.exp(spread * noise) if base else spread * noise
        out[name] = jnp.asarray(drawn.astype(out[name].dtype))
    for name, factor in factors.items():
        out[name] = (out[name] * factor).astype(out[name].dtype)
    return out
```

```python
from contextlib import ExitStack

import concourse.bass as bass
from concourse import mybir

F32 = mybir.dt.float32
F32R = mybir.dt.float32r
BF16 = mybir.dt.bfloat16
ALU = mybir.AluOpType
ACT = mybir.ActivationFunctionType

P = 128
Q = 32
NQ = P // Q
NL = 512
LB = NL // Q
XT_BANKS = 2
Y_BANKS = 4
SLOTS = 4
RING = 4
WARM = 14


def build(nc, x, cond, w, bvec, out):
    B, L, D = x.shape
    C = cond.shape[1]
    NK = D // P
    H = L // NL
    G = B * H
    CK = C // P
    assert D == NK * P and D == NQ * NK * Q and H == 2 and w.shape == (3 * D, D) and 2 * C == D
    every = tuple(range(NK))
    EW = C // NQ

    xv = x.rearrange("b (h lb lm) (j e) -> (b h) j lm lb e", h=H, lm=Q, j=NQ)
    ov = out.rearrange("b (h lb lm) (j e) -> (b h) j lm lb e", h=H, lm=Q, j=NQ)
    wv = w[0:2 * D, :].rearrange("(s j k m) o -> s j m k o", s=2, j=NQ, m=Q)
    w3v = w[2 * D:3 * D, :].rearrange("(r j k m) o -> r j m k o", r=2, j=NQ, m=Q)

    with ExitStack() as ctx:
        def sb(name, shape, dt=F32):
            return ctx.enter_context(nc.sbuf_tensor(name, shape, dt))

        def psum(name, shape):
            return ctx.enter_context(nc.psum_tensor(name, shape, F32))

        def sem(name):
            return ctx.enter_context(nc.semaphore(name))

        xa = sb("xa", [P, G, LB, P])
        w1 = sb("w1", [P, NK, D])
        w2 = sb("w2", [P, NK, D])
        w3 = sb("w3", [P, 2, CK, D])
        w3sum = sb("w3sum", [P, CK, NK, P])
        w2x = sb("w2x", [P, NK, NK, P])
        ones = sb("ones", [P, 1])
        w1h = sb("w1h", [P, NK, NK, P], F32R)
        w1l = sb("w1l", [P, NK, NK, P], F32R)
        xh = sb("xh", [P, SLOTS, NK, NL], F32R)
        xl = sb("xl", [P, SLOTS, NK, NL], F32R)
        relu_t = sb("relu_t", [P, RING, NL])
        back = sb("back", [P, RING, LB, Q])
        cond_a = sb("cond_a", [P, EW])
        cond_t = sb("cond_t", [P, CK, Q])
        b_a = sb("b_a", [P, P])
        b_t = sb("b_t", [P, NK, Q])
        xsum = sb("xsum", [P, H, NK])
        bsum = sb("bsum", [P, NK])
        const_bias = sb("const_bias", [P, NK, B])
        bias = sb("bias", [P, NK])
        warm = sb("warm", [P, NL], BF16)

        ps_xt = psum("ps_xt", [P, XT_BANKS, NL])
        ps_y = psum("ps_y", [P, Y_BANKS, NL])
        ps_b = psum("ps_b", [P, NL])
        ps_const = ps_b[:, 0:NK * B].rearrange("p (k b) -> p k b", k=NK)
        ps_mean = ps_b[:, NK * B:NK * B + NK]

        x_landed = [sem(f"x_landed{h}") for h in range(H)]
        w1_landed = [sem(f"w1_landed{k}") for k in range(2)]
        w2_landed, w3_landed, small_landed = sem("w2_landed"), sem("w3_landed"), sem("small_landed")
        stored = sem("stored")
        warm_zeroed, small_zeroed, ones_set = sem("warm_zeroed"), sem("small_zeroed"), sem("ones_set")
        w2x_ready, w2x_paired, w2x_summed = sem("w2x_ready"), sem("w2x_paired"), sem("w2x_summed")
        w1h_ready, w1l_ready, w3_added = sem("w1h_ready"), sem("w1l_ready"), sem("w3_added")
        small_turned, const_summed, const_ready = sem("small_turned"), sem("const_summed"), sem("const_ready")
        bsum_ready, mean_done, bias_ready = sem("bsum_ready"), sem("mean_done"), sem("bias_ready")
        xt_ready, xh_ready, xl_ready = sem("xt_ready"), sem("xh_ready"), sem("xl_ready")
        y_ready = sem("y_ready")
        relu_done, turned_back, added = sem("relu_done"), sem("turned_back"), sem("added")

        def load_x(eng, g, h, quadrants):
            for j in quadrants:
                eng.dma_start(xa[Q * j:Q * j + Q, g], xv[g, j]).then_inc(x_landed[h], 16)

        def load_w1(eng, half, quadrants):
            ks = slice(half * NK // 2, (half + 1) * NK // 2)
            for j in quadrants:
                eng.dma_start(w1[Q * j:Q * j + Q, ks], wv[0, j, :, ks]).then_inc(w1_landed[half], 16)

        block = ctx.enter_context(nc.Block())

        @block.sync
        def _(sp):
            load_x(sp, 0, 0, (0, 1))
            load_w1(sp, 0, (0, 1))
            load_w1(sp, 1, (0, 1))
            load_x(sp, 1, 1, (0, 1))
            sp.wait_ge(small_zeroed, 2)
            for j in range(NQ):
                sp.dma_start(cond_a[Q * j:Q * j + B, :], cond[:, EW * j:EW * j + EW]).then_inc(small_landed, 16)
                sp.dma_start(b_a[Q * j:Q * j + 1, :],
                             bvec[P * j:P * j + P].rearrange("(a e) -> a e", a=1)).then_inc(small_landed, 16)
            for j in range(NQ):
                for r in range(2):
                    sp.dma_start(w3[Q * j:Q * j + Q, r], w3v[r, j]).then_inc(w3_landed, 16)
            for j in range(NQ):
                sp.dma_start(w2[Q * j:Q * j + Q], wv[1, j]).then_inc(w2_landed, 16)
            with sp.Fori(1, B) as b:
                for h in range(H):
                    sp.wait_ge(x_landed[h], 16 * NQ * b)
                    for j in range(NQ):
                        sp.dma_start(xa[Q * j:Q * j + Q, H * b + h], xv[H * b + h, j]).then_inc(x_landed[h], 16)
            with sp.Fori(0, G) as g:
                sp.wait_ge(added, NK * g + NK)
                for j in range(NQ):
                    sp.dma_start(ov[g, j], xa[Q * j:Q * j + Q, g]).then_inc(stored, 16)
            sp.wait_ge(stored, 16 * NQ * G)

        @block.gpsimd
        def _(pool):
            nc.gpsimd.memset(warm[:], 0.0).then_inc(warm_zeroed, 1)
            nc.gpsimd.memset(cond_a[:], 0.0).then_inc(small_zeroed, 1)
            nc.gpsimd.memset(b_a[:], 0.0).then_inc(small_zeroed, 1)
            nc.gpsimd.memset(ones[:], 1.0).then_inc(ones_set, 1)
            for k in range(NK):
                pool.wait_ge(w1_landed[k // 2], 16 * NQ)
                pool.wait_ge(w1h_ready, k + 1)
                nc.gpsimd.tensor_tensor(w1l[:, k].rearrange("p t (j m) -> p t j m", j=NQ),
                                        w1[:, k].rearrange("p (j t m) -> p t j m", j=NQ, t=NK),
                                        w1h[:, k].rearrange("p t (j m) -> p t j m", j=NQ),
                                        ALU.subtract).then_inc(w1l_ready, 1)
            pool.wait_ge(w3_landed, 16 * NQ * 2)
            for k in range(CK):
                nc.gpsimd.tensor_tensor(w3sum[:, k].rearrange("p t (j m) -> p t j m", j=NQ),
                                        w3[:, 0, k].rearrange("p (j t m) -> p t j m", j=NQ, t=NK),
                                        w3[:, 1, k].rearrange("p (j t m) -> p t j m", j=NQ, t=NK),
                                        ALU.add).then_inc(w3_added, 1)

            def batch_sum(b):
                pool.wait_ge(xh_ready, H * NK * b + H * NK)
                nc.gpsimd.tensor_tensor(bsum[:], xsum[:, 0], xsum[:, 1], ALU.add).then_inc(bsum_ready, 1)

            def mean_terms(b):
                pool.wait_ge(w2x_ready, NK * b + NK)
                nc.gpsimd.tensor_tensor(w2x[:, 0:2], w2x[:, 0:2], w2x[:, 2:4], ALU.add).then_inc(w2x_paired, 1)
                pool.wait_ge(w2x_paired, b + 1)
                nc.gpsimd.tensor_tensor(w2x[:, 0], w2x[:, 0], w2x[:, 1], ALU.add).then_inc(w2x_summed, 1)

            def residual(g, tiles):
                for t in tiles:
                    pool.wait_ge(turned_back, NK * g + t + 1)
                    rows = xa[:, g, :, Q * t:Q * t + Q]
                    nc.gpsimd.tensor_tensor(rows, rows, back[:, t % RING], ALU.add).then_inc(added, 1)

            batch_sum(0)
            mean_terms(0)
            with pool.Fori(0, B - 1) as b:
                residual(H * b, every)
                residual(H * b + 1, every[:-1])
                batch_sum(b + 1)
                residual(H * b + 1, every[-1:])
                mean_terms(b + 1)
            residual(G - 2, every)
            residual(G - 1, every)

        @block.scalar
        def _(act):
            load_x(act, 0, 0, (2, 3))
            load_w1(act, 0, (2, 3))
            load_w1(act, 1, (2, 3))
            load_x(act, 1, 1, (2, 3))

            def w1_high(k):
                act.wait_ge(w1_landed[k // 2], 16 * NQ)
                nc.scalar.activation(w1h[:, k].rearrange("p t (j m) -> p t j m", j=NQ),
                                     w1[:, k].rearrange("p (j t m) -> p t j m", j=NQ, t=NK),
                                     ACT.Copy).then_inc(w1h_ready, 1)

            def x_high(g, h, slot, k):
                act.wait_ge(xt_ready, NK * g + k + 1)
                nc.scalar.activation(xh[:, slot, k], ps_xt[:, k % XT_BANKS],
                                     ACT.Copy, accum_out=xsum[:, h, k:k + 1]).then_inc(xh_ready, 1)

            def mean_rows(b):
                if not (isinstance(b, int) and b == 0):
                    act.wait_ge(mean_done, b)
                act.wait_ge(bsum_ready, b + 1)
                for k in range(NK):
                    nc.scalar.activation(w2x[:, k].rearrange("p t (j m) -> p t j m", j=NQ),
                                         w2[:, k].rearrange("p (j t m) -> p t j m", j=NQ, t=NK),
                                         ACT.Copy, scale=bsum[:, k:k + 1]).then_inc(w2x_ready, 1)

            def relu(g, t):
                act.wait_ge(y_ready, NK * g + t + 1)
                nc.scalar.activation(relu_t[:, t % RING], ps_y[:, t % Y_BANKS], ACT.Relu,
                                     bias=bias[:, t:t + 1]).then_inc(relu_done, 1)

            for k in range(NK):
                w1_high(k)
                x_high(0, 0, 0, k)
            for k in range(NK):
                x_high(1, 1, 1, k)
            act.wait_ge(w2_landed, 16 * NQ)
            mean_rows(0)

            def steps(b, more):
                for h in range(H):
                    g = H * b + h
                    if h == 0:
                        act.wait_ge(bias_ready, b + 1)
                    for t in range(NK):
                        if not (isinstance(g, int) and NK * g + t < RING):
                            act.wait_ge(turned_back, NK * g + t + 1 - RING)
                        relu(g, t)
                        if more:
                            x_high(g + 2, h, (g + 2) % SLOTS, t)

                if more:
                    mean_rows(b + 1)

            steps(0, True)
            with act.Fori(1, B - 1) as b:
                steps(b, True)
            steps(B - 1, False)

        @block.vector
        def _(dve):
            def turn_x(g, h, k):
                if NK * g + k >= XT_BANKS:
                    dve.wait_ge(xl_ready, NK * g + k + 1 - XT_BANKS)
                nc.vector.transpose(ps_xt[:, k % XT_BANKS].rearrange("p (lb lm) -> p lb lm", lm=Q),
                                    xa[:, g, :, Q * k:Q * k + Q]).then_inc(xt_ready, 1)

            def x_low(g, slot, k):
                dve.wait_ge(xh_ready, NK * g + k + 1)
                nc.vector.tensor_tensor(xl[:, slot, k], ps_xt[:, k % XT_BANKS], xh[:, slot, k],
                                        ALU.subtract).then_inc(xl_ready, 1)

            def turn_back(g, t):
                dve.wait_ge(relu_done, NK * g + t + 1)
                nc.vector.transpose(back[:, t % RING], relu_t[:, t % RING].rearrange("p (lb om) -> p lb om", om=Q)
                                    ).then_inc(turned_back, 1)

            def sum_bias(b):
                if b > 0:
                    dve.wait_ge(relu_done, H * NK * b)
                dve.wait_ge(mean_done, b + 1)
                nc.vector.scalar_tensor_tensor(out=bias[:], in0=ps_mean, scalar=1.0 / L, in1=const_bias[:, :, b],
                                               op0=ALU.mult, op1=ALU.add).then_inc(bias_ready, 1)

            for g in range(2):
                dve.wait_ge(x_landed[g], 16 * NQ)
                turn_x(g, g, 0)
                for k in range(NK):
                    if k + 1 < NK:
                        turn_x(g, g, k + 1)
                    x_low(g, g, k)
            dve.wait_ge(small_landed, 16 * NQ * 2)
            nc.vector.transpose(cond_t[:], cond_a[:].rearrange("p (k b) -> p k b", b=Q)).then_inc(small_turned, 1)
            nc.vector.transpose(b_t[:], b_a[:].rearrange("p (k b) -> p k b", b=Q)).then_inc(small_turned, 1)
            dve.wait_ge(const_summed, 1)
            dve.wait_ge(small_turned, 2)
            nc.vector.tensor_tensor(const_bias[:], ps_const, b_t[:, :, 0:1].to_broadcast([P, NK, B]),
                                    ALU.add).then_inc(const_ready, 1)
            dve.wait_ge(const_ready, 1)
            sum_bias(0)

            def steps(b, more):
                for h in range(H):
                    g = H * b + h
                    for t in range(NK):
                        if more:
                            if t == 0:
                                dve.wait_ge(x_landed[h], 16 * NQ * (b + 2))
                                turn_x(g + 2, h, 0)
                        if NK * g + t >= RING:
                            dve.wait_ge(added, NK * g + t + 1 - RING)
                        turn_back(g, t)
                        if more:
                            if t + 1 < NK:
                                turn_x(g + 2, h, t + 1)
                            x_low(g + 2, (g + 2) % SLOTS, t)
                if more:
                    sum_bias(b + 1)

            for b in range(B):
                steps(b, b + 1 < B)

        @block.tensor
        def _(pe):
            pe.wait_ge(warm_zeroed, 1)
            for _i in range(WARM):
                nc.tensor.matmul(ps_b[:], warm[:, 0:P], warm[:], start=True, stop=True)

            def product(slot, k, t):
                y = ps_y[:, t % Y_BANKS]
                nc.tensor.matmul(y, w1h[:, k, t], xh[:, slot, k], start=(k == 0), stop=False, skip_group_check=True)
                nc.tensor.matmul(y, w1h[:, k, t], xl[:, slot, k], start=False, stop=False, skip_group_check=True)
                return nc.tensor.matmul(y, w1l[:, k, t], xh[:, slot, k], start=False, stop=(k == NK - 1),
                                        skip_group_check=True)

            def group(g, slot, tiles):
                for t in tiles:
                    pe.wait_ge(relu_done, NK * g + t + 1 - Y_BANKS)
                    for k in range(NK):
                        if t == 0:
                            pe.wait_ge(xl_ready, NK * g + k + 1)
                        last = product(slot, k, t)
                    last.then_inc(y_ready, 1)

            def mean_bias(b):
                pe.wait_ge(w2x_summed, b + 1)
                for t in range(NK):
                    last = nc.tensor.matmul(ps_mean[:, t:t + 1], w2x[:, 0, t], ones[:], start=True, stop=True)
                last.then_inc(mean_done, 1)

            for k in range(NK):
                pe.wait_ge(xl_ready, k + 1)
                pe.wait_ge(w1l_ready, k + 1)
                for t in range(NK):
                    last = product(0, k, t)
                    if k == NK - 1:
                        last.then_inc(y_ready, 1)
            pe.wait_ge(small_turned, 1)
            pe.wait_ge(w3_added, CK)
            for t in range(NK):
                for k in range(CK):
                    last = nc.tensor.matmul(ps_const[:, t], w3sum[:, k, t], cond_t[:, k, 0:B], start=(k == 0), stop=(k == CK - 1))
            last.then_inc(const_summed, 1)
            pe.wait_ge(ones_set, 1)
            pe.wait_ge(const_ready, 1)
            mean_bias(0)

            with pe.Fori(0, B - 1) as b:
                group(H * b + 1, (H * b + 1) % SLOTS, every)
                group(H * b + 2, (H * b + 2) % SLOTS, every[:NK // 2])
                pe.wait_ge(bias_ready, b + 1)
                mean_bias(b + 1)
                group(H * b + 2, (H * b + 2) % SLOTS, every[NK // 2:])
            group(G - 1, (G - 1) % SLOTS, every)


_INS = ['x', 'cond_512', 'L0_cond_W', 'L0_cond_b']
_OUTS = [((4, 1024, 512), 'float32')]


def kernel(**inputs):
    import numpy as _np
    import concourse.bacc as _bacc
    from concourse import mybir as _mybir
    from concourse.bass_utils import run_bass_kernel_spmd as _run

    nc = _bacc.Bacc("TRN2", target_bir_lowering=False, num_devices=1)
    arrays, args = {}, []
    for name in _INS:
        a = _np.ascontiguousarray(inputs[name])
        arrays[f"in_{name}_dram"] = a
        args.append(nc.dram_tensor(f"in_{name}_dram", a.shape, _mybir.dt.from_np(a.dtype), kind="ExternalInput").ap())
    for i, (shape, dtype) in enumerate(_OUTS):
        dt = _mybir.dt.from_np(_np.dtype(dtype))
        args.append(nc.dram_tensor(f"out_{i}_dram", shape, dt, kind="ExternalOutput").ap())
    build(nc, *args)
    r = _run(nc, [arrays], core_ids=[0])
    return r.results[0]["out_0_dram"]
```

```python
from contextlib import ExitStack

import concourse.bass as bass
from concourse import mybir

F32 = mybir.dt.float32
F32R = mybir.dt.float32r
BF16 = mybir.dt.bfloat16
ALU = mybir.AluOpType
ACT = mybir.ActivationFunctionType

P = 128
Q = 32
NQ = P // Q
NL = 512
HL = NL // 2
LB = NL // Q
XT_BANKS = 2
Y_BANKS = 4
SLOTS = 4
RING = 4
WARM = 14


def build(nc, x, cond, w, bvec, out):
    B, L, D = x.shape
    C = cond.shape[1]
    NK = D // P
    H = L // NL
    G = B * H
    CK = C // P
    LAST = G - 1
    assert D == NK * P and D == NQ * NK * Q and H == 2 and w.shape == (3 * D, D) and 2 * C == D
    assert NK % XT_BANKS == 0 and NK == Y_BANKS == RING

    pieces = [(0, l, HL, k) for l in (0, HL) for k in range(NK)]
    pieces += [(g, 0, NL, k) for g in range(1, G) for k in range(NK)]

    def pieces_to(g):
        return NK * g + NK * (g > 0 if isinstance(g, int) else 1)

    tiles = [(g, 0, NL, t) for g in range(LAST) for t in range(NK)]
    tiles += [(LAST, l, HL, t) for l in (0, HL) for t in range(NK)]

    def steps_of_x(n):
        g, _l, _nl, t = tiles[n]
        if g == 0:
            return 2 if t < NK // 2 else 0
        return 1 if g + SLOTS - 1 < G else 0

    xv = x.rearrange("b (h lb lm) (j e) -> (b h) j lm lb e", h=H, lm=Q, j=NQ)
    ov = out.rearrange("b (h lb lm) (j e) -> (b h) j lm lb e", h=H, lm=Q, j=NQ)
    wv = w[0:2 * D, :].rearrange("(s j k m) o -> s j m k o", s=2, j=NQ, m=Q)
    w3v = w[2 * D:3 * D, :].rearrange("(r p k) o -> r p k o", r=2, k=CK)
    cv = cond.rearrange("b (p k) -> p b k", k=CK)

    def by_tile(rows):
        return rows.rearrange("p (j t m) -> p t j m", j=NQ, t=NK)

    def as_tiles(rows):
        return rows.rearrange("p t (j m) -> p t j m", j=NQ)

    with ExitStack() as ctx:
        def sb(name, shape, dt=F32):
            return ctx.enter_context(nc.sbuf_tensor(name, shape, dt))

        def psum(name, shape):
            return ctx.enter_context(nc.psum_tensor(name, shape, F32))

        def sem(name):
            return ctx.enter_context(nc.semaphore(name))

        xa = sb("xa", [P, G, LB, P])
        w1 = sb("w1", [P, NK, D])
        w2 = sb("w2", [P, NK, D])
        w3 = sb("w3", [P, 2, CK, D])
        w3sum = sb("w3sum", [P, CK, D])
        w2x = sb("w2x", [P, NK, D])
        ones = sb("ones", [P, P])
        w1h = sb("w1h", [P, NK, NK, P], F32R)
        w1l = sb("w1l", [P, NK, NK, P], F32R)
        xh = sb("xh", [P, SLOTS, NK, NL], F32R)
        xl = sb("xl", [P, SLOTS, NK, NL], F32R)
        relu_t = sb("relu_t", [P, RING, NL])
        back = sb("back", [P, RING, LB, Q])
        cond_c = sb("cond_c", [P, B, CK])
        cond_t = sb("cond_t", [P, CK, NQ, Q])
        b_row = sb("b_row", [P, D])
        xsum = sb("xsum", [P, G + 1, NK])
        bsum = sb("bsum", [P, NK])
        const_row = sb("const_row", [P, P])
        bias_row = sb("bias_row", [P, P])
        bias = sb("bias", [P, B, NK, Q])
        warm = sb("warm", [P, NL], BF16)
        act_warm = sb("act_warm", [P, 1])

        ps_xt = psum("ps_xt", [P, XT_BANKS, NL])
        ps_y = psum("ps_y", [P, Y_BANKS, NL])
        ps_b = psum("ps_b", [P, D])

        x0_landed = [sem(f"x0_landed{h}") for h in range(2)]
        x_landed = [sem(f"x_landed{h}") for h in range(H)]
        w1_landed = [sem(f"w1_landed{k}") for k in range(2)]
        w1_q23_landed = [sem(f"w1_q23_landed{k}") for k in range(2)]
        w2_landed, w3_landed, small_landed = sem("w2_landed"), sem("w3_landed"), sem("small_landed")
        stored = sem("stored")
        warm_zeroed, cond_zeroed, ones_set = sem("warm_zeroed"), sem("cond_zeroed"), sem("ones_set")
        w1h_ready, w1l_ready, w3_added = sem("w1h_ready"), sem("w1l_ready"), sem("w3_added")
        cond_spread, const_summed, const_ready = sem("cond_spread"), sem("const_summed"), sem("const_ready")
        halves_summed, bsum_ready = sem("halves_summed"), sem("bsum_ready")
        w2x_ready, w2x_paired, w2x_summed = sem("w2x_ready"), sem("w2x_paired"), sem("w2x_summed")
        mean_done, bias_summed, bias_ready = sem("mean_done"), sem("bias_summed"), sem("bias_ready")
        xt_ready, xh_ready, xl_ready = sem("xt_ready"), sem("xh_ready"), sem("xl_ready")
        y_ready, y_saved, relu_done = sem("y_ready"), sem("y_saved"), sem("relu_done")
        turned_back, added = sem("turned_back"), sem("added")

        def load_x0(eng, half):
            lbs = slice(half * LB // 2, (half + 1) * LB // 2)
            for j in range(NQ):
                eng.dma_start(xa[Q * j:Q * j + Q, 0, lbs], xv[0, j, :, lbs]).then_inc(x0_landed[half], 16)

        def load_w1(eng, half, quadrants, landed):
            ks = slice(half * NK // 2, (half + 1) * NK // 2)
            for j in quadrants:
                eng.dma_start(w1[Q * j:Q * j + Q, ks], wv[0, j, :, ks]).then_inc(landed[half], 16)

        block = ctx.enter_context(nc.Block())

        @block.sync
        def _(sp):
            def load_x(g, h):
                for j in range(NQ):
                    sp.dma_start(xa[Q * j:Q * j + Q, g], xv[g, j]).then_inc(x_landed[h], 16)

            load_x0(sp, 0)
            load_w1(sp, 1, range(0, 2), w1_landed)
            load_x0(sp, 1)
            load_x(1, 1)
            sp.dma_start(cond_c[:], cv).then_inc(small_landed, 16)
            sp.dma_start(b_row[:], bvec.partition_broadcast(P)).then_inc(small_landed, 16)
            for j in range(NQ):
                sp.dma_start(w2[Q * j:Q * j + Q], wv[1, j]).then_inc(w2_landed, 16)
            for r in range(2):
                sp.dma_start(w3[:, r], w3v[r]).then_inc(w3_landed, 16)
            load_x(2, 0)
            with sp.Fori(1, B - 1) as b:
                sp.wait_ge(x_landed[1], 16 * NQ * b)
                load_x(H * b + 1, 1)
                sp.wait_ge(x_landed[0], 16 * NQ * b)
                load_x(H * b + 2, 0)
            sp.wait_ge(x_landed[1], 16 * NQ * (B - 1))
            load_x(LAST, 1)
            with sp.Fori(0, LAST) as g:
                sp.wait_ge(added, NK * g + NK)
                for j in range(NQ):
                    sp.dma_start(ov[g, j], xa[Q * j:Q * j + Q, g]).then_inc(stored, 16)
            for half in range(2):
                sp.wait_ge(added, NK * (LAST + half + 1))
                lbs = slice(half * LB // 2, (half + 1) * LB // 2)
                for j in range(NQ):
                    sp.dma_start(ov[LAST, j, :, lbs], xa[Q * j:Q * j + Q, LAST, lbs]).then_inc(stored, 16)
            sp.wait_ge(stored, 16 * NQ * (G + 1))

        @block.gpsimd
        def _(pool):
            load_w1(pool, 0, range(2, NQ), w1_q23_landed)
            load_w1(pool, 1, range(2, NQ), w1_q23_landed)
            nc.gpsimd.memset(cond_t[:], 0.0).then_inc(cond_zeroed, 1)
            for k in range(NK):
                pool.wait_ge(w1_landed[k // 2], 16 * NQ // 2)
                pool.wait_ge(w1_q23_landed[k // 2], 16 * NQ // 2)
                pool.wait_ge(w1h_ready, k + 1)
                nc.gpsimd.tensor_tensor(as_tiles(w1l[:, k]), by_tile(w1[:, k]), as_tiles(w1h[:, k]),
                                        ALU.subtract).then_inc(w1l_ready, 1)

            def mean_terms(b):
                for n in range(2):
                    pool.wait_ge(w2x_ready, NK * b + 2 * n + 2)
                    nc.gpsimd.tensor_tensor(w2x[:, 2 * n], w2x[:, 2 * n], w2x[:, 2 * n + 1], ALU.add
                                            ).then_inc(w2x_paired, 1)
                pool.wait_ge(w2x_paired, 2 * b + 2)
                nc.gpsimd.tensor_tensor(w2x[:, 0], w2x[:, 0], w2x[:, 2], ALU.add).then_inc(w2x_summed, 1)

            def residual(g, t, n, lbs=slice(0, LB)):
                pool.wait_ge(turned_back, n)
                rows = xa[:, g, lbs, Q * t:Q * t + Q]
                nc.gpsimd.tensor_tensor(rows, rows, back[:, t % RING, 0:lbs.stop - lbs.start], ALU.add).then_inc(added, 1)

            pool.wait_ge(small_landed, 16 * 2)
            pool.wait_ge(cond_zeroed, 1)
            for j in range(NQ):
                nc.gpsimd.tensor_copy(cond_t[:, :, j, 0:B], cond_c[:].rearrange("p b k -> p k b")).then_inc(cond_spread, 1)
            pool.wait_ge(w3_landed, 16 * 2)
            nc.gpsimd.tensor_tensor(w3sum[:], w3[:, 0], w3[:, 1], ALU.add).then_inc(w3_added, 1)
            mean_terms(0)
            for t in range(NK):
                residual(0, t, t + 1)
            mean_terms(1)
            with pool.Fori(1, B - 1) as b:
                for t in range(NK):
                    residual(H * b - 1, t, NK * (H * b - 1) + t + 1)
                for t in range(NK):
                    residual(H * b, t, NK * H * b + t + 1)
                mean_terms(b + 1)
            for n, (g, l, nl, t) in enumerate(tiles):
                if g >= G - H - 1:
                    residual(g, t, n + 1, slice(l // Q, (l + nl) // Q))

        @block.scalar
        def _(act):
            load_w1(act, 0, range(0, 2), w1_landed)
            act.wait_ge(ones_set, 1)
            nc.scalar.activation(act_warm[:], ones[:, 0:1], ACT.Relu)

            def w1_high(k):
                act.wait_ge(w1_landed[k // 2], 16 * NQ // 2)
                act.wait_ge(w1_q23_landed[k // 2], 16 * NQ // 2)
                nc.scalar.activation(as_tiles(w1h[:, k]), by_tile(w1[:, k]), ACT.Copy).then_inc(w1h_ready, 1)

            def x_high(n):
                g, l, nl, k = pieces[n]
                part = g + 1 if g else l // HL
                act.wait_ge(xt_ready, n + 1)
                nc.scalar.activation(xh[:, g % SLOTS, k, l:l + nl], ps_xt[:, n % XT_BANKS, 0:nl], ACT.Copy,
                                     accum_out=xsum[:, part, k:k + 1]).then_inc(xh_ready, 1)

            def mean_row(k):
                nc.scalar.activation(w2x[:, k], w2[:, k], ACT.Copy, scale=bsum[:, k:k + 1]).then_inc(w2x_ready, 1)

            def mean_rows(b):
                act.wait_ge(mean_done, b)
                act.wait_ge(bsum_ready, b + 1)
                for k in range(NK):
                    mean_row(k)

            def save(n):
                act.wait_ge(y_ready, n + 1)
                nc.scalar.activation(relu_t[:, n], ps_y[:, n], ACT.Copy).then_inc(y_saved, 1)

            def relu(n):
                g, l, nl, t = tiles[n]
                products = ps_y[:, t, l:l + nl]
                if g == 0:
                    act.wait_ge(y_saved, n + 1)
                    products = relu_t[:, t]
                else:
                    act.wait_ge(y_ready, n + 1)
                    act.wait_ge(turned_back, n + 1 - RING)
                nc.scalar.activation(relu_t[:, t, 0:nl], products, ACT.Relu,
                                     bias=bias[:, g // H, t, g // H:g // H + 1]).then_inc(relu_done, 1)

            mean_at = [NK + 1] + [NK * H * (b - 1) + NK - 1 for b in range(2, B)]
            for k in range(NK):
                x_high(k)
                w1_high(k)
            for n in range(NK, pieces_to(H)):
                x_high(n)
            act.wait_ge(bsum_ready, 1)
            act.wait_ge(w2_landed, 16 * NQ)
            n_x = pieces_to(H)
            for k in range(NK):
                x_high(n_x + k)
                save(k)
                mean_row(k)
            n_x += NK
            for n, (g, l, nl, t) in enumerate(tiles):
                if n % (H * NK) == 0 and l == 0:
                    act.wait_ge(bias_ready, g // H + 1)
                relu(n)
                for _n in range(steps_of_x(n)):
                    x_high(n_x)
                    n_x += 1
                if n in mean_at:
                    mean_rows(mean_at.index(n) + 1)

        @block.vector
        def _(dve):
            def turn_x(n):
                g, l, nl, k = pieces[n]
                if k == 0:
                    if g == 0:
                        dve.wait_ge(x0_landed[l // HL], 16 * NQ)
                    else:
                        dve.wait_ge(x_landed[g % H], 16 * NQ * ((g + 1) // H))
                if n >= XT_BANKS:
                    dve.wait_ge(xl_ready, n + 1 - XT_BANKS)
                nc.vector.transpose(ps_xt[:, n % XT_BANKS, 0:nl],
                                    xa[:, g, l // Q:(l + nl) // Q, Q * k:Q * k + Q]).then_inc(xt_ready, 1)

            def x_low(n):
                g, l, nl, k = pieces[n]
                dve.wait_ge(xh_ready, n + 1)
                nc.vector.tensor_tensor(xl[:, g % SLOTS, k, l:l + nl], ps_xt[:, n % XT_BANKS, 0:nl],
                                        xh[:, g % SLOTS, k, l:l + nl], ALU.subtract).then_inc(xl_ready, 1)

            def turn_back(n):
                g, l, nl, t = tiles[n]
                dve.wait_ge(relu_done, n + 1)
                if n >= RING:
                    dve.wait_ge(added, n + 1 - RING)
                nc.vector.transpose(back[:, t, 0:nl // Q], relu_t[:, t, 0:nl].rearrange("p (lb om) -> p lb om", om=Q)
                                    ).then_inc(turned_back, 1)

            def batch_sum(b):
                if b == 0:
                    nc.vector.tensor_tensor(xsum[:, 1], xsum[:, 0], xsum[:, 1], ALU.add).then_inc(halves_summed, 1)
                    dve.wait_ge(halves_summed, 1)
                else:
                    dve.wait_ge(w2x_ready, NK * b)
                nc.vector.tensor_tensor(bsum[:], xsum[:, H * b + 1], xsum[:, H * b + 2], ALU.add).then_inc(bsum_ready, 1)

            def sum_bias(b):
                dve.wait_ge(mean_done, b + 1)
                for j in range(NQ):
                    rows, cols = slice(Q * j, Q * j + Q), slice(P * j, P * j + P)
                    nc.vector.scalar_tensor_tensor(out=bias_row[rows], in0=ps_b[rows, cols], scalar=1.0 / L, in1=const_row[rows],
                                                   op0=ALU.mult, op1=ALU.add).then_inc(bias_summed, 1)
                dve.wait_ge(bias_summed, NQ * (b + 1))
                nc.vector.transpose(bias[:, b], bias_row[:].rearrange("p (t b) -> p t b", b=Q)).then_inc(bias_ready, 1)

            def turn_and_split(first, end):
                for n in range(first, end):
                    early = n + 1 < end and pieces[n + 1][3] > 0
                    if early:
                        turn_x(n + 1)
                    x_low(n)
                    if n + 1 < end and not early:
                        turn_x(n + 1)

            nc.vector.memset(warm[:], 0.0).then_inc(warm_zeroed, 1)
            nc.vector.memset(ones[:], 1.0).then_inc(ones_set, 1)
            turn_x(0)
            turn_and_split(0, pieces_to(H))
            batch_sum(0)
            turn_x(pieces_to(H))
            turn_and_split(pieces_to(H), pieces_to(H + 1))
            dve.wait_ge(const_summed, 1)
            dve.wait_ge(small_landed, 16 * 2)
            for j in range(NQ):
                rows, cols = slice(Q * j, Q * j + Q), slice(P * j, P * j + P)
                nc.vector.tensor_tensor(const_row[rows], ps_b[rows, cols], b_row[rows, cols], ALU.add).then_inc(const_ready, 1)
            n_x = pieces_to(H + 1)
            dve.wait_ge(const_ready, NQ)
            sum_bias(0)
            turn_x(n_x)
            for n, (g, l, nl, t) in enumerate(tiles):
                turn_back(n)
                if n % (H * NK) == H * NK - 1 and g // H + 1 < B:
                    sum_bias(g // H + 1)
                for _n in range(steps_of_x(n)):
                    if n_x + 1 < len(pieces):
                        turn_x(n_x + 1)
                    x_low(n_x)
                    n_x += 1
                    g_next = pieces[n_x - 1][0]
                    if n_x == pieces_to(g_next + 1) and g_next % H == H - 1:
                        batch_sum(g_next // H)

        @block.tensor
        def _(pe):
            pe.wait_ge(warm_zeroed, 1)
            for _n in range(WARM):
                nc.tensor.matmul(ps_b[:], warm[:, 0:P], warm[:], start=True, stop=True)

            def mm(t, ls, lhs, rhs, start=False, stop=False):
                return nc.tensor.matmul(ps_y[:, t, ls], lhs, rhs, start=start, stop=stop, skip_group_check=True)

            def product(slot, k, t, ls=slice(0, NL)):
                mm(t, ls, w1h[:, k, t], xh[:, slot, k, ls], start=(k == 0))
                mm(t, ls, w1h[:, k, t], xl[:, slot, k, ls])
                return mm(t, ls, w1l[:, k, t], xh[:, slot, k, ls], stop=(k == NK - 1))

            def tile(g, slot, t):
                for k in range(NK):
                    if t == 0:
                        pe.wait_ge(xl_ready, pieces_to(g) + k + 1)
                    last = product(slot, k, t)
                last.then_inc(y_ready, 1)

            def mean_bias(b):
                pe.wait_ge(w2x_summed, b + 1)
                nc.tensor.matmul(ps_b[:], ones[:], w2x[:, 0], start=True, stop=True).then_inc(mean_done, 1)

            for half in range(2):
                ls = slice(half * HL, (half + 1) * HL)
                for k in range(NK):
                    pe.wait_ge(xl_ready, NK * half + k + 1)
                    if half == 0:
                        pe.wait_ge(w1h_ready, k + 1)
                    for t in range(NK):
                        mm(t, ls, w1h[:, k, t], xh[:, 0, k, ls], start=(half == 0 and k == 0))
                        mm(t, ls, w1h[:, k, t], xl[:, 0, k, ls])
            for t in range(NK):
                for k in range(NK):
                    if t == 0:
                        pe.wait_ge(w1l_ready, k + 1)
                    last = mm(t, slice(0, NL), w1l[:, k, t], xh[:, 0, k], stop=(k == NK - 1))
                last.then_inc(y_ready, 1)
            pe.wait_ge(cond_spread, NQ)
            pe.wait_ge(w3_added, 1)
            for k in range(CK):
                last = nc.tensor.matmul(ps_b[:], cond_t[:, k].rearrange("p j b -> p (j b)"), w3sum[:, k],
                                        start=(k == 0), stop=(k == CK - 1))
            last.then_inc(const_summed, 1)
            for t in range(NK):
                pe.wait_ge(y_saved, t + 1)
                tile(1, 1, t)
                if t == 1:
                    pe.wait_ge(const_ready, NQ)
                    mean_bias(0)

            def even_group(b):
                for t in range(NK):
                    pe.wait_ge(relu_done, NK * (H * b - 1) + t + 1)
                    tile(H * b, (H * b) % SLOTS, t)
                    if t == 2:
                        pe.wait_ge(bias_ready, b)
                        mean_bias(b)

            with pe.Fori(1, B - 1) as b:
                even_group(b)
                for t in range(NK):
                    pe.wait_ge(relu_done, NK * H * b + t + 1)
                    tile(H * b + 1, (H * b + 1) % SLOTS, t)
            even_group(B - 1)
            for n, (g, l, nl, t) in enumerate(tiles):
                if g == LAST:
                    pe.wait_ge(relu_done, n + 1 - Y_BANKS)
                    for k in range(NK):
                        if n == NK * LAST:
                            pe.wait_ge(xl_ready, pieces_to(g) + k + 1)
                        last = product(g % SLOTS, k, t, slice(l, l + nl))
                    last.then_inc(y_ready, 1)


_INS = ['x', 'cond_512', 'L0_cond_W', 'L0_cond_b']
_OUTS = [((4, 1024, 512), 'float32')]


def kernel(**inputs):
    import numpy as _np
    import concourse.bacc as _bacc
    from concourse import mybir as _mybir
    from concourse.bass_utils import run_bass_kernel_spmd as _run

    nc = _bacc.Bacc("TRN2", target_bir_lowering=False, num_devices=1)
    arrays, args = {}, []
    for name in _INS:
        a = _np.ascontiguousarray(inputs[name])
        arrays[f"in_{name}_dram"] = a
        args.append(nc.dram_tensor(f"in_{name}_dram", a.shape, _mybir.dt.from_np(a.dtype), kind="ExternalInput").ap())
    for i, (shape, dtype) in enumerate(_OUTS):
        dt = _mybir.dt.from_np(_np.dtype(dtype))
        args.append(nc.dram_tensor(f"out_{i}_dram", shape, dt, kind="ExternalOutput").ap())
    build(nc, *args)
    r = _run(nc, [arrays], core_ids=[0])
    return r.results[0]["out_0_dram"]
```

```python
from contextlib import ExitStack

import concourse.bass as bass
from concourse import mybir

F32 = mybir.dt.float32
F32R = mybir.dt.float32r
BF16 = mybir.dt.bfloat16
ALU = mybir.AluOpType
ACT = mybir.ActivationFunctionType

P = 128
Q = 32
NQ = P // Q
NL = 512
HL = NL // 2
LB = NL // Q
XT_BANKS = 2
Y_BANKS = 4
SLOTS = 4
RELU_RING = 8
BACK_RING = 4
WARM = 14


def build(nc, x, cond, w, bvec, out):
    B, L, D = x.shape
    C = cond.shape[1]
    NK = D // P
    H = L // NL
    G = B * H
    CK = C // P
    LAST = G - 1
    assert D == NK * P and D == NQ * NK * Q and H == 2 and w.shape == (3 * D, D) and 2 * C == D
    assert NK % XT_BANKS == 0 and NK == Y_BANKS == BACK_RING and RELU_RING == H * NK

    pieces = [(0, l, HL, k) for l in (0, HL) for k in range(NK)]
    pieces += [(g, 0, NL, k) for g in range(1, G) for k in range(NK)]

    def pieces_to(g):
        return NK * g + NK * (g > 0 if isinstance(g, int) else 1)

    tiles = [(g, 0, NL, t) for g in range(LAST) for t in range(NK)]
    tiles += [(LAST, l, HL, t) for l in (0, HL) for t in range(NK)]

    def steps_of_x(n, ahead):
        return 1 if SLOTS <= tiles[n][0] + ahead < G else 0

    xv = x.rearrange("b (h lb lm) (j e) -> (b h) j lm lb e", h=H, lm=Q, j=NQ)
    ov = out.rearrange("b (h lb lm) (j e) -> (b h) j lm lb e", h=H, lm=Q, j=NQ)
    wv = w[0:2 * D, :].rearrange("(s j k m) o -> s j m k o", s=2, j=NQ, m=Q)
    w3v = w[2 * D:3 * D, :].rearrange("(r p k) o -> r p k o", r=2, k=CK)
    cv = cond.rearrange("b (p k) -> p b k", k=CK)

    def by_tile(rows):
        return rows.rearrange("p (j t m) -> p t j m", j=NQ, t=NK)

    def as_tiles(rows):
        return rows.rearrange("p t (j m) -> p t j m", j=NQ)

    with ExitStack() as ctx:
        def sb(name, shape, dt=F32):
            return ctx.enter_context(nc.sbuf_tensor(name, shape, dt))

        def psum(name, shape):
            return ctx.enter_context(nc.psum_tensor(name, shape, F32))

        def sem(name):
            return ctx.enter_context(nc.semaphore(name))

        xa = sb("xa", [P, G, LB, P])
        w1 = sb("w1", [P, NK, D])
        w2 = sb("w2", [P, NK, D])
        w3 = sb("w3", [P, 2, CK, D])
        w3sum = sb("w3sum", [P, CK, D])
        w2x = sb("w2x", [P, D])
        ones = sb("ones", [P, P])
        w1h = sb("w1h", [P, NK, NK, P], F32R)
        w1l = sb("w1l", [P, NK, NK, P], F32R)
        xh = sb("xh", [P, SLOTS, NK, NL], F32R)
        xl = sb("xl", [P, SLOTS, NK, NL], F32R)
        relu_t = sb("relu_t", [P, RELU_RING, NL])
        back = sb("back", [P, BACK_RING, LB, Q])
        cond_c = sb("cond_c", [P, B, CK])
        cond_t = sb("cond_t", [P, CK, NQ, Q])
        b_row = sb("b_row", [P, D])
        xsum = sb("xsum", [P, G + 1, NK])
        bsum = sb("bsum", [P, NK])
        const_row = sb("const_row", [P, P])
        bias_row = sb("bias_row", [P, P])
        bias = sb("bias", [P, B, NK, Q])
        warm = sb("warm", [P, NL], BF16)
        act_warm = sb("act_warm", [P, 1])

        ps_xt = psum("ps_xt", [P, XT_BANKS, NL])
        ps_y = psum("ps_y", [P, Y_BANKS, NL])
        ps_const = psum("ps_const", [P, D])
        ps_mean = psum("ps_mean", [P, D])

        x0_landed = [sem(f"x0_landed{h}") for h in range(2)]
        x_landed = [sem(f"x_landed{h}") for h in range(H)]
        w1_landed = [sem(f"w1_landed{k}") for k in range(2)]
        w1_q23_landed = [sem(f"w1_q23_landed{k}") for k in range(2)]
        w2_landed, w3_landed = sem("w2_landed"), sem("w3_landed")
        cond_landed, b_landed = sem("cond_landed"), sem("b_landed")
        stored = sem("stored")
        warm_zeroed, cond_zeroed, ones_set = sem("warm_zeroed"), sem("cond_zeroed"), sem("ones_set")
        w1h_ready, w1l_ready, w3_added = sem("w1h_ready"), sem("w1l_ready"), sem("w3_added")
        cond_spread, const_summed, const_ready = sem("cond_spread"), sem("const_summed"), sem("const_ready")
        halves_summed, bsum_ready = sem("halves_summed"), sem("bsum_ready")
        w2x_step = sem("w2x_step")
        mean_done, bias_summed, bias_ready = sem("mean_done"), sem("bias_summed"), sem("bias_ready")
        xt_ready, xh_ready, xl_ready = sem("xt_ready"), sem("xh_ready"), sem("xl_ready")
        y_ready, y_saved, relu_done = sem("y_ready"), sem("y_saved"), sem("relu_done")
        turned_back, added, last_added = sem("turned_back"), sem("added"), sem("last_added")

        def load_x0(eng, half):
            lbs = slice(half * LB // 2, (half + 1) * LB // 2)
            for j in range(NQ):
                eng.dma_start(xa[Q * j:Q * j + Q, 0, lbs], xv[0, j, :, lbs]).then_inc(x0_landed[half], 16)

        def load_w1(eng, half, quadrants, landed):
            ks = slice(half * NK // 2, (half + 1) * NK // 2)
            for j in quadrants:
                eng.dma_start(w1[Q * j:Q * j + Q, ks], wv[0, j, :, ks]).then_inc(landed[half], 16)

        def store_last(eng, quadrants):
            for half in range(2):
                eng.wait_ge(last_added, NK * (half + 1))
                lbs = slice(half * LB // 2, (half + 1) * LB // 2)
                for j in quadrants:
                    eng.dma_start(ov[LAST, j, :, lbs], xa[Q * j:Q * j + Q, LAST, lbs]).then_inc(stored, 16)

        block = ctx.enter_context(nc.Block())

        @block.sync
        def _(sp):
            def load_x(g, h):
                for j in range(NQ):
                    sp.dma_start(xa[Q * j:Q * j + Q, g], xv[g, j]).then_inc(x_landed[h], 16)

            load_x0(sp, 0)
            load_w1(sp, 1, range(0, 2), w1_landed)
            load_x0(sp, 1)
            load_x(1, 1)
            sp.dma_start(cond_c[:], cv).then_inc(cond_landed, 16)
            for j in range(NQ):
                sp.dma_start(w2[Q * j:Q * j + Q], wv[1, j]).then_inc(w2_landed, 16)
            for r in range(2):
                sp.dma_start(w3[:, r], w3v[r]).then_inc(w3_landed, 16)
            sp.dma_start(b_row[:], bvec.partition_broadcast(P)).then_inc(b_landed, 16)
            load_x(2, 0)
            with sp.Fori(1, B - 1) as b:
                sp.wait_ge(x_landed[1], 16 * NQ * b)
                load_x(H * b + 1, 1)
                sp.wait_ge(x_landed[0], 16 * NQ * b)
                load_x(H * b + 2, 0)
            sp.wait_ge(x_landed[1], 16 * NQ * (B - 1))
            load_x(LAST, 1)
            with sp.Fori(0, LAST) as g:
                sp.wait_ge(added, NK * g + NK)
                for j in range(NQ):
                    sp.dma_start(ov[g, j], xa[Q * j:Q * j + Q, g]).then_inc(stored, 16)
            store_last(sp, range(0, 2))
            sp.wait_ge(stored, 16 * (NQ * LAST + 2 * NQ))

        @block.gpsimd
        def _(pool):
            load_w1(pool, 0, range(2, NQ), w1_q23_landed)
            load_w1(pool, 1, range(2, NQ), w1_q23_landed)
            nc.gpsimd.memset(cond_t[:], 0.0).then_inc(cond_zeroed, 1)
            for k in range(NK):
                pool.wait_ge(w1_landed[k // 2], 16 * NQ // 2)
                pool.wait_ge(w1_q23_landed[k // 2], 16 * NQ // 2)
                pool.wait_ge(w1h_ready, k + 1)
                nc.gpsimd.tensor_tensor(as_tiles(w1l[:, k]), by_tile(w1[:, k]), as_tiles(w1h[:, k]),
                                        ALU.subtract).then_inc(w1l_ready, 1)

            def residual(g, t, n):
                pool.wait_ge(turned_back, n)
                rows = xa[:, g, :, Q * t:Q * t + Q]
                nc.gpsimd.tensor_tensor(rows, rows, back[:, t], ALU.add).then_inc(added, 1)

            pool.wait_ge(cond_landed, 16)
            pool.wait_ge(cond_zeroed, 1)
            for j in range(NQ):
                nc.gpsimd.tensor_copy(cond_t[:, :, j, 0:B], cond_c[:].rearrange("p b k -> p k b")).then_inc(cond_spread, 1)
            pool.wait_ge(w3_landed, 16 * 2)
            nc.gpsimd.tensor_tensor(w3sum[:], w3[:, 0], w3[:, 1], ALU.add).then_inc(w3_added, 1)
            with pool.Fori(0, LAST) as g:
                for t in range(NK):
                    residual(g, t, NK * g + t + 1)

        @block.scalar
        def _(act):
            load_w1(act, 0, range(0, 2), w1_landed)
            act.wait_ge(ones_set, 1)
            nc.scalar.activation(act_warm[:], ones[:, 0:1], ACT.Relu)

            def w1_high(k):
                act.wait_ge(w1_landed[k // 2], 16 * NQ // 2)
                act.wait_ge(w1_q23_landed[k // 2], 16 * NQ // 2)
                nc.scalar.activation(as_tiles(w1h[:, k]), by_tile(w1[:, k]), ACT.Copy).then_inc(w1h_ready, 1)

            def x_high(n):
                g, l, nl, k = pieces[n]
                part = g + 1 if g else l // HL
                act.wait_ge(xt_ready, n + 1)
                nc.scalar.activation(xh[:, g % SLOTS, k, l:l + nl], ps_xt[:, n % XT_BANKS, 0:nl], ACT.Copy,
                                     accum_out=xsum[:, part, k:k + 1]).then_inc(xh_ready, 1)

            def save(n):
                act.wait_ge(y_ready, n + 1)
                nc.scalar.activation(relu_t[:, n % RELU_RING], ps_y[:, n], ACT.Copy).then_inc(y_saved, 1)

            def relu(n):
                g, l, nl, t = tiles[n]
                products, slot = ps_y[:, t, l:l + nl], n % RELU_RING
                if g == 0:
                    act.wait_ge(y_saved, n + 1)
                    products = relu_t[:, slot]
                else:
                    act.wait_ge(y_ready, n + 1)
                    if n >= RELU_RING:
                        act.wait_ge(turned_back, n + 1 - RELU_RING)
                if n % (H * NK) == 0 and l == 0:
                    act.wait_ge(bias_ready, g // H + 1)
                nc.scalar.activation(relu_t[:, slot, 0:nl], products, ACT.Relu,
                                     bias=bias[:, g // H, t, g // H:g // H + 1]).then_inc(relu_done, 1)

            w1_high(0)
            w1_high(1)
            x_high(0)
            x_high(1)
            for k in range(2, NK):
                w1_high(k)
                x_high(k)
            x_beside = (1, 0, 1, 1, 0, 2, 1, 1)
            n_x = pieces_to(H) + 1
            assert n_x + sum(x_beside) == pieces_to(SLOTS)
            for n in range(NK, n_x):
                if n == pieces_to(H) - 1:
                    save(0)
                if n == n_x - 1:
                    for t in range(1, NK):
                        save(t)
                x_high(n)
            for n in range(len(tiles)):
                for _n in range(x_beside[n] if n < H * NK else 0):
                    x_high(n_x)
                    n_x += 1
                relu(n)
                for _n in range(steps_of_x(n, 2)):
                    x_high(n_x)
                    n_x += 1
            store_last(act, range(2, NQ))

        @block.vector
        def _(dve):
            def turn_x(n):
                g, l, nl, k = pieces[n]
                if k == 0:
                    if g == 0:
                        dve.wait_ge(x0_landed[l // HL], 16 * NQ)
                    else:
                        dve.wait_ge(x_landed[g % H], 16 * NQ * ((g + 1) // H))
                if n >= XT_BANKS:
                    dve.wait_ge(xl_ready, n + 1 - XT_BANKS)
                nc.vector.transpose(ps_xt[:, n % XT_BANKS, 0:nl],
                                    xa[:, g, l // Q:(l + nl) // Q, Q * k:Q * k + Q]).then_inc(xt_ready, 1)

            def x_low(n):
                g, l, nl, k = pieces[n]
                dve.wait_ge(xh_ready, n + 1)
                nc.vector.tensor_tensor(xl[:, g % SLOTS, k, l:l + nl], ps_xt[:, n % XT_BANKS, 0:nl],
                                        xh[:, g % SLOTS, k, l:l + nl], ALU.subtract).then_inc(xl_ready, 1)

            def turn_back(n):
                g, l, nl, t = tiles[n]
                dve.wait_ge(relu_done, n + 1)
                if n >= BACK_RING:
                    if n < NK * LAST + BACK_RING:
                        dve.wait_ge(added, n + 1 - BACK_RING)
                    else:
                        dve.wait_ge(last_added, n + 1 - BACK_RING - NK * LAST)
                nc.vector.transpose(back[:, t, 0:nl // Q], relu_t[:, n % RELU_RING, 0:nl].rearrange("p (lb om) -> p lb om", om=Q)
                                    ).then_inc(turned_back, 1)

            def mean_terms(b):
                if b == 0:
                    nc.vector.tensor_tensor(xsum[:, 1], xsum[:, 0], xsum[:, 1], ALU.add).then_inc(halves_summed, 1)
                    dve.wait_ge(w2_landed, 16 * NQ)
                    dve.wait_ge(halves_summed, 1)
                else:
                    dve.wait_ge(mean_done, b)
                    dve.wait_ge(w2x_step, NK * b)
                nc.vector.tensor_tensor(bsum[:], xsum[:, H * b + 1], xsum[:, H * b + 2], ALU.add).then_inc(bsum_ready, 1)
                dve.wait_ge(bsum_ready, b + 1)
                nc.vector.tensor_scalar(w2x[:], w2[:, 0], bsum[:, 0:1], None, ALU.mult).then_inc(w2x_step, 1)
                for k in range(1, NK):
                    dve.wait_ge(w2x_step, NK * b + k)
                    nc.vector.scalar_tensor_tensor(out=w2x[:], in0=w2[:, k], scalar=bsum[:, k:k + 1], in1=w2x[:],
                                                   op0=ALU.mult, op1=ALU.add).then_inc(w2x_step, 1)

            def residual(n):
                g, l, nl, t = tiles[n]
                dve.wait_ge(turned_back, n + 1)
                rows = xa[:, g, l // Q:(l + nl) // Q, Q * t:Q * t + Q]
                nc.vector.tensor_tensor(rows, rows, back[:, t, 0:nl // Q], ALU.add).then_inc(last_added, 1)

            def sum_bias(b):
                dve.wait_ge(mean_done, b + 1)
                for j in range(NQ):
                    rows, cols = slice(Q * j, Q * j + Q), slice(P * j, P * j + P)
                    nc.vector.scalar_tensor_tensor(out=bias_row[rows], in0=ps_mean[rows, cols], scalar=1.0 / L, in1=const_row[rows],
                                                   op0=ALU.mult, op1=ALU.add).then_inc(bias_summed, 1)
                dve.wait_ge(bias_summed, NQ * (b + 1))
                nc.vector.transpose(bias[:, b], bias_row[:].rearrange("p (t b) -> p t b", b=Q)).then_inc(bias_ready, 1)

            def turn_and_split(first, end):
                for n in range(first, end):
                    early = n + 1 < end and pieces[n + 1][3] > 0
                    if early:
                        turn_x(n + 1)
                    x_low(n)
                    if n + 1 < end and not early:
                        turn_x(n + 1)

            nc.vector.memset(warm[:], 0.0).then_inc(warm_zeroed, 1)
            nc.vector.memset(ones[:], 1.0).then_inc(ones_set, 1)
            turn_x(0)
            turn_and_split(0, pieces_to(H))
            mean_terms(0)
            n_x = pieces_to(H)
            turn_x(n_x)
            turn_and_split(n_x, n_x + 1)
            dve.wait_ge(const_summed, 1)
            dve.wait_ge(b_landed, 16)
            for j in range(NQ):
                rows, cols = slice(Q * j, Q * j + Q), slice(P * j, P * j + P)
                nc.vector.tensor_tensor(const_row[rows], ps_const[rows, cols], b_row[rows, cols], ALU.add).then_inc(const_ready, 1)
            dve.wait_ge(const_ready, NQ)
            sum_bias(0)
            turn_x(n_x + 1)
            turn_and_split(n_x + 1, pieces_to(SLOTS))
            mean_terms(1)
            n_x = pieces_to(SLOTS)
            for n, (g, l, nl, t) in enumerate(tiles):
                if t == 0 and l == 0:
                    if g % H == H - 1 and g // H + 1 < B - 1:
                        sum_bias(g // H + 1)
                    elif g == H * (B - 1):
                        sum_bias(B - 1)
                turn_back(n)
                if g == LAST:
                    residual(n)
                for _n in range(steps_of_x(n, 3)):
                    if t == 0:
                        turn_x(n_x)
                    if t < NK - 1:
                        turn_x(n_x + 1)
                    x_low(n_x)
                    n_x += 1
                if g + SLOTS - 1 < G and g > 0 and g % H == 0 and t == NK - 1:
                    mean_terms(g // H + 1)

        @block.tensor
        def _(pe):
            pe.wait_ge(warm_zeroed, 1)
            for _n in range(WARM):
                nc.tensor.matmul(ps_mean[:], warm[:, 0:P], warm[:], start=True, stop=True)

            def mm(t, ls, lhs, rhs, start=False, stop=False):
                return nc.tensor.matmul(ps_y[:, t, ls], lhs, rhs, start=start, stop=stop, skip_group_check=True)

            def product(slot, k, t, ls=slice(0, NL)):
                mm(t, ls, w1h[:, k, t], xh[:, slot, k, ls], start=(k == 0))
                mm(t, ls, w1h[:, k, t], xl[:, slot, k, ls])
                return mm(t, ls, w1l[:, k, t], xh[:, slot, k, ls], stop=(k == NK - 1))

            def tile(g, slot, t):
                for k in range(NK):
                    if t == 0:
                        pe.wait_ge(xl_ready, pieces_to(g) + k + 1)
                    last = product(slot, k, t)
                last.then_inc(y_ready, 1)

            def mean_bias(b):
                pe.wait_ge(w2x_step, NK * b + NK)
                nc.tensor.matmul(ps_mean[:], ones[:], w2x[:], start=True, stop=True).then_inc(mean_done, 1)

            for half in range(2):
                ls = slice(half * HL, (half + 1) * HL)
                for k in range(NK):
                    pe.wait_ge(xh_ready, NK * half + k + 1)
                    if half == 0:
                        pe.wait_ge(w1h_ready, k + 1)
                    for t in range(NK):
                        mm(t, ls, w1h[:, k, t], xh[:, 0, k, ls], start=(half == 0 and k == 0))
                    pe.wait_ge(xl_ready, NK * half + k + 1)
                    for t in range(NK):
                        mm(t, ls, w1h[:, k, t], xl[:, 0, k, ls])
            for t in range(NK):
                for k in range(NK):
                    if t == 0:
                        pe.wait_ge(w1l_ready, k + 1)
                    last = mm(t, slice(0, NL), w1l[:, k, t], xh[:, 0, k], stop=(k == NK - 1))
                last.then_inc(y_ready, 1)
            for t in range(NK):
                pe.wait_ge(y_saved, t + 1)
                tile(1, 1, t)
                if t == 0:
                    pe.wait_ge(cond_spread, NQ)
                    pe.wait_ge(w3_added, 1)
                    for k in range(CK):
                        last = nc.tensor.matmul(ps_const[:], cond_t[:, k].rearrange("p j b -> p (j b)"), w3sum[:, k],
                                                start=(k == 0), stop=(k == CK - 1))
                    last.then_inc(const_summed, 1)
                    mean_bias(0)

            def even_group(b):
                for t in range(NK):
                    pe.wait_ge(relu_done, NK * (H * b - 1) + t + 1)
                    tile(H * b, (H * b) % SLOTS, t)
                    if t == 2:
                        pe.wait_ge(bias_ready, b)
                        mean_bias(b)

            with pe.Fori(1, B - 1) as b:
                even_group(b)
                for t in range(NK):
                    pe.wait_ge(relu_done, NK * H * b + t + 1)
                    tile(H * b + 1, (H * b + 1) % SLOTS, t)
            even_group(B - 1)
            for n, (g, l, nl, t) in enumerate(tiles):
                if g == LAST:
                    pe.wait_ge(relu_done, n + 1 - Y_BANKS)
                    for k in range(NK):
                        if n == NK * LAST:
                            pe.wait_ge(xl_ready, pieces_to(g) + k + 1)
                        last = product(g % SLOTS, k, t, slice(l, l + nl))
                    last.then_inc(y_ready, 1)


_INS = ['x', 'cond_512', 'L0_cond_W', 'L0_cond_b']
_OUTS = [((4, 1024, 512), 'float32')]


def kernel(**inputs):
    import numpy as _np
    import concourse.bacc as _bacc
    from concourse import mybir as _mybir
    from concourse.bass_utils import run_bass_kernel_spmd as _run

    nc = _bacc.Bacc("TRN2", target_bir_lowering=False, num_devices=1)
    arrays, args = {}, []
    for name in _INS:
        a = _np.ascontiguousarray(inputs[name])
        arrays[f"in_{name}_dram"] = a
        args.append(nc.dram_tensor(f"in_{name}_dram", a.shape, _mybir.dt.from_np(a.dtype), kind="ExternalInput").ap())
    for i, (shape, dtype) in enumerate(_OUTS):
        dt = _mybir.dt.from_np(_np.dtype(dtype))
        args.append(nc.dram_tensor(f"out_{i}_dram", shape, dt, kind="ExternalOutput").ap())
    build(nc, *args)
    r = _run(nc, [arrays], core_ids=[0])
    return r.results[0]["out_0_dram"]
```
